# Optimizing a Trainium2 kernel written in Bass

```python
import numpy as np
import jax
import jax.numpy as jnp

def _softmax(x, axis=-1):
    return jax.nn.softmax(x, axis=axis)

def _gelu(x):
    return jax.nn.gelu(x, approximate=True)

def _silu(x):
    return jax.nn.silu(x)

def _sigmoid(x):
    return jax.nn.sigmoid(x)

def _layernorm(x, axis=-1, eps=1e-05):
    m = jnp.mean(x, axis=axis, keepdims=True)
    v = jnp.var(x, axis=axis, keepdims=True)
    return (x - m) / jnp.sqrt(v + eps)

def _scatter_add(tgt, idx, src, axis=0):
    return tgt.at[idx].add(src)

def _segment_sum(src, seg, n):
    return jax.ops.segment_sum(src, seg, n)
kernel_name = 'mk_adj_resnorm_d1_adj_r2_5ab0a3'

def setup_inputs(seed: int=0):
    np.random.seed(seed)
    _w = jnp.asarray

    def _rec_inputs():
        import jax
        import jax.numpy as jnp
        _gk = jax.random.key(seed)
        x = -0.0002928 + 1 * jax.random.normal(jax.random.fold_in(_gk, 1), (8192, 256), jnp.float32)
        _a = jax.random.bernoulli(jax.random.fold_in(_gk, 2), 0.00195312, (8192, 8192))
        _a = jnp.logical_or(_a, jnp.swapaxes(_a, -1, -2))
        _a = jnp.logical_or(_a, jnp.eye(8192, dtype=bool))
        _af = _a.astype(jnp.float32)
        _af = _af * jax.random.uniform(jax.random.fold_in(_gk, 3), (8192, 8192), jnp.float32, 0.05, 1)
        adj = _af
        return (x, adj)
    x, adj = _rec_inputs()

    def _L0_gnn_setup():
        import jax, jax.numpy as jnp
        import numpy as np
        EPS = 1e-08
        key = jax.random.key(seed)
        k1, k2, k3, k4 = jax.random.split(key, 4)
        N, IN, OUT = (4096, 256, 256)
        x = jax.random.normal(k1, (N, IN), dtype=jnp.float32)
        adj = jax.random.uniform(k2, (N, N), dtype=jnp.float32)
        W = jax.random.normal(k3, (OUT, IN), dtype=jnp.float32) * (1.0 / np.sqrt(IN))
        b = jax.random.normal(k4, (OUT,), dtype=jnp.float32) * 0.01
        return {'x': x, 'adj': adj, 'W': W, 'b': b}
    _L0_gnn_all = _L0_gnn_setup()
    _L0_gnn_in = {k: v for k, v in _L0_gnn_all.items() if k in ('W', 'b')}
    del _L0_gnn_all
    return {'x': x, 'adj': adj, 'L0_gnn_W': _L0_gnn_in['W'], 'L0_gnn_b': _L0_gnn_in['b']}

def reference(x, adj, L0_gnn_W, L0_gnn_b):
    import jax
    import jax.numpy as jnp

    def _L0_gnn_ref(x, adj, W, b):
        import jax, jax.numpy as jnp
        import numpy as np
        EPS = 1e-08
        deg = adj.sum(axis=1)
        dis = (deg + EPS) ** (-0.5)
        a_norm = dis[:, None] * adj * dis[None, :]
        h = a_norm @ x
        return h @ W.T + b
    x = _layernorm(x + _L0_gnn_ref(x, adj, L0_gnn_W, L0_gnn_b), axis=-1)
    return x

_drawn_inputs = setup_inputs


def setup_inputs(seed=0):
    import zlib

    import numpy as np

    out = dict(_drawn_inputs(seed))
    spreads = {}
    factors = {'L0_gnn_b': 6.272}
    for name, (base, spread) in spreads.items():
        noise = np.random.default_rng([zlib.crc32(name.encode()), seed]).standard_normal(out[name].shape)
        drawn = base * np.exp(spread * noise) if base else spread * noise
        out[name] = jnp.asarray(drawn.astype(out[name].dtype))
    for name, factor in factors.items():
        out[name] = (out[name] * factor).astype(out[name].dtype)
    return out
```

```python
import concourse.bass as bass
from concourse import mybir
from concourse.alu_op_type import AluOpType as ALU
from contextlib import ExitStack

F32 = mybir.dt.float32
F32R = mybir.dt.float32r
ACT = mybir.ActivationFunctionType
AX_X = mybir.AxisListType.X

P = 128
N = 8192
D = 256
Q = 32
PANELS = N // P
TILES = 8
CHUNKS = PANELS // TILES
GROUPS = CHUNKS
CW = TILES * P
QUARTERS = 4
QW = N // QUARTERS
QT = QW // P
ROWGROUPS = P // Q
RING = 3
DEG_EPS = 1e-8
NORM_EPS = 1e-5

FIRST_CHUNKS = TILES * sum(range(GROUPS))
FIRST_PANELS = PANELS - TILES
TURN = CHUNKS + 1
FOLD_AFTER = 0
SPREAD_AFTER, SAVE_AFTER, DEGREES_AFTER, Y_AFTER = 0, 1, 2, 5


def dve_sums(g):
    return (0, 2) if g <= 2 else (0,) if g == 3 else ()


def split_by(g, k):
    return -(-(k + 1) * g // QUARTERS)


def rows_base(g):
    return TILES * sum(range(g))


def cols_base(g):
    return FIRST_CHUNKS + TILES * TURN * g


def ring_slot(t, period):
    return 1 if period > 1 and period % RING == 1 and t == period - 1 else t % RING


def ring_distances():
    periods = [("rows", g, g) for g in range(1, GROUPS)] + [("cols", g, TURN) for g in range(GROUPS // 2)]
    used, n, found = {}, 0, {}
    for sweep, g, period in periods:
        least = [RING] * period
        for _ in range(TILES):
            for t in range(period):
                slot = ring_slot(t, period)
                least[t] = min(least[t], n - used.get(slot, -RING))
                used[slot] = n
                n += 1
        found[sweep, g] = least
    return found


def gnn_kernel(nc, adj_rows, adj_cols, x, x_t, w_t, bias, out, partial):
    x_panels = x.rearrange("(n p) d -> n p d", p=P)
    out_panels = out.rearrange("(n p) d -> n p d", p=P)

    ctx = ExitStack()
    with ctx:
        def sb(name, shape, dt=F32):
            return ctx.enter_context(nc.sbuf_tensor(name, shape, dt))

        def sem(name):
            return ctx.enter_context(nc.semaphore(name))

        raw = sb("raw", [P, QUARTERS, QW])
        tr = sb("tr", [P, 2, CW])
        hi = sb("hi", [P, RING, CW], F32R)
        lo = sb("lo", [P, RING, CW], F32R)
        y = sb("y", [P, PANELS, 2 * D], F32R)
        wt_sb = sb("wt_sb", [P, 2, D])
        xt_sb = sb("xt_sb", [P, 2, P])
        bias_sb = sb("bias_sb", [P, D])
        same_row = sb("same_row", [P, Q])
        minus_half = sb("minus_half", [P, 1])
        ones = sb("ones", [P, 1])
        sums = sb("sums", [P, 2, QUARTERS, ROWGROUPS])
        row_sum = sb("row_sum", [P, ROWGROUPS])
        spread = sb("spread", [P, ROWGROUPS, Q])
        deg_col = sb("deg_col", [P, 1])
        dis = sb("dis", [P, PANELS])
        spill = sb("spill", [P, D])
        raw_more = sb("raw_more", [P, CW])
        res = tr[:, 0, :].rearrange("p (i j d) -> p i j d", i=2, j=2)
        part = tr[:, 1, :].rearrange("p (i j d) -> p i j d", i=2, j=2)
        z = sb("z", [P, 2, D])
        stats = sb("stats", [P, 6])
        mean_var = sb("mean_var", [P, 2])
        var_eps = sb("var_eps", [P, 1])
        rstd = sb("rstd", [P, 1])

        prod = ctx.enter_context(nc.psum_tensor("prod", [P, 2, 2 * D], F32))
        y_ps = ctx.enter_context(nc.psum_tensor("y_ps", [P, 2 * D], F32))
        deg_ps = ctx.enter_context(nc.psum_tensor("deg_ps", [P, 2 * D], F32))
        unused = ctx.enter_context(nc.psum_tensor("unused", [P, ROWGROUPS, QW // ROWGROUPS], F32))

        rows_in = [sem(f"rows_in{k}") for k in range(QUARTERS)]
        cols_in = [sem(f"cols_in{k}") for k in range(TURN)]
        const_in = sem("const_in")
        xt_in = sem("xt_in")
        res_in = sem("res_in")
        consts_made = sem("consts_made")
        summed = [sem(f"summed{k}") for k in range(QUARTERS)]
        transposed = sem("transposed")
        hi_done = sem("hi_done")
        lo_done = sem("lo_done")
        chunk_used = sem("chunk_used")
        row_sum_done = sem("row_sum_done")
        spread_done = sem("spread_done")
        fold_done = sem("fold_done")
        deg_done = sem("deg_done")
        dis_done = sem("dis_done")
        y_ps_done = sem("y_ps_done")
        y_hi_done = sem("y_hi_done")
        y_done = sem("y_done")
        half_read = sem("half_read")
        prod_read = sem("prod_read")
        spill_out = sem("spill_out")
        res_done = sem("res_done")
        z_done = sem("z_done")
        stats_done = sem("stats_done")
        mean_var_done = sem("mean_var_done")
        var_done = sem("var_done")
        rstd_done = sem("rstd_done")
        out_done = sem("out_done")
        out_stored = [sem(f"out_stored{j}") for j in range(2)]

        block = ctx.enter_context(nc.Block())

        def wait_apart(eng, semaphore, count):
            eng.compute_val(count)
            eng.wait_ge(consts_made, 3 + ROWGROUPS)
            eng.wait_ge(semaphore, count)

        def raw_chunk(slot):
            return raw[:, slot // 2, slot % 2 * CW:(slot % 2 + 1) * CW] if slot < CHUNKS else raw_more[:, :]

        distances = ring_distances()

        def turn_chunk(g, t):
            return (0, g + t) if t < CHUNKS - g else (1, t - 1)

        def turn_panels(g, i):
            return g * TILES + i, (GROUPS - 1 - g) * TILES + i

        def res_loads(g, i):
            return (3 * TILES if g > 0 else 0) + max(g - 1, 0) * 4 * TILES + (4 if g > 0 else 3) * (i + 1)

        @block.sync
        def _(sp):
            def load_quarter(p, k):
                sp.dma_start(raw[:, k, :], adj_rows[p, k, :, :]).then_inc(rows_in[k], 16)

            def wait_quarter_used(g, p, q, k):
                wait_apart(sp, summed[k], p + 1)
                if g > 2 * k:
                    wait_apart(sp, transposed, rows_base(g) + q * g + min(g, 2 * k + 2))

            for k in range(QUARTERS):
                load_quarter(0, k)
            for g in range(GROUPS):
                last = g == GROUPS - 1
                with sp.Fori(0, TILES - 1 if last else TILES) as q:
                    p = g * TILES + q
                    for k in range(QUARTERS):
                        wait_quarter_used(g, p, q, k)
                        load_quarter(p + 1, k)

            def load_chunk(g, i, t):
                j, c = turn_chunk(g, t)
                sp.dma_start(raw_chunk(t), adj_cols[turn_panels(g, i)[j], c, :, :]).then_inc(cols_in[t], 16)

            def load_res(g, i):
                turn = g * TILES + i
                if not isinstance(turn, int) or turn > 0:
                    wait_apart(sp, res_in, 16 * res_loads(g, i - 1))
                if not isinstance(turn, int) or turn > 1:
                    wait_apart(sp, z_done, 2 * turn - 2)
                for j, p in enumerate(turn_panels(g, i)):
                    sp.dma_start(res[:, i % 2, j, :], x_panels[p, :, :]).then_inc(res_in, 16)
                    if g > 0 or j > 0:
                        sp.dma_start(part[:, i % 2, j, :], partial[p, :, :]).then_inc(res_in, 16)

            load_chunk(0, 0, TURN - 1)
            for t in range(CHUNKS):
                if t % 2 == 0:
                    wait_quarter_used(GROUPS - 1, PANELS - 1, TILES - 1, t // 2)
                load_chunk(0, 0, t)
            sp.wait_ge(lo_done, FIRST_CHUNKS)
            sp.wait_ge(spill_out, 16 * FIRST_PANELS)
            load_res(0, 0)

            def load_turn(g, i):
                for t in range(TURN):
                    wait_apart(sp, lo_done, cols_base(g) + (i - 1) * TURN + t + 1)
                    load_chunk(g, i, t)
                    if t == 2:
                        load_res(g, i)

            load_turn(0, 1)
            for g in range(GROUPS // 2):
                with sp.Fori(2 if g == 0 else 0, TILES) as i:
                    load_turn(g, i)

        @block.gpsimd
        def _(pool):
            pool.dma_start(wt_sb[:, :, :], w_t).then_inc(const_in, 16)
            pool.dma_start(bias_sb[:, :], bias).then_inc(const_in, 16)
            pool.dma_start(xt_sb[:, :, :], x_t[0, :, :, :]).then_inc(xt_in, 16)
            pool.memset(minus_half[:, :], -0.5).then_inc(consts_made, 1)
            pool.memset(ones[:, :], 1.0).then_inc(consts_made, 1)
            pool.memset(same_row[:, :], 0.0).then_inc(consts_made, 1)
            for a in range(ROWGROUPS):
                pool.wait_ge(consts_made, 3 + a)
                pool.affine_select(out=same_row[:, :], in_=same_row[:, :], compare_op=ALU.not_equal, fill=1.0,
                                   base=-Q * a, pattern=[[-1, Q]], channel_multiplier=1).then_inc(consts_made, 1)

            def powers(p):
                wait_apart(pool, deg_done, p + 1)
                pool.tensor_tensor(dis[:, bass.ds(p, 1)], deg_col[:, :], minus_half[:, :], ALU.pow)\
                    .then_inc(dis_done, 1)

            def store_partial(p):
                pool.wait_ge(prod_read, p - TILES + 1)
                pool.dma_start(partial[p, :, :], spill[:, :]).then_inc(spill_out, 16)

            def load_xt(p):
                pool.wait_ge(y_ps_done, p)
                pool.dma_start(xt_sb[:, :, :], x_t[p, :, :, :]).then_inc(xt_in, 16)

            with pool.Fori(1, TILES + 1) as p:
                powers(p - 1)
                load_xt(p)
            with pool.Fori(TILES + 1, PANELS) as p:
                powers(p - 1)
                load_xt(p)
                store_partial(p - 1)
            powers(PANELS - 1)
            store_partial(PANELS - 1)

            def add_bias(g, i):
                wait_apart(pool, res_in, 16 * res_loads(g, i))
                for j in range(2):
                    pool.tensor_tensor(res[:, i % 2, j, :], res[:, i % 2, j, :], bias_sb[:, :], ALU.add)\
                        .then_inc(res_done, 1)

            def finish(g, i):
                for j, p in enumerate(turn_panels(g, i)):
                    done = 2 * (g * TILES + i) + j + 1
                    pool.wait_ge(var_done, done)
                    pool.tensor_tensor(rstd[:, :], var_eps[:, :], minus_half[:, :], ALU.pow).then_inc(rstd_done, 1)
                    pool.wait_ge(out_done, done)
                    pool.dma_start(out_panels[p, :, :], z[:, j, :]).then_inc(out_stored[j], 16)

            for g in range(GROUPS // 2):
                with pool.Fori(0, TILES) as i:
                    add_bias(g, i)
                    finish(g, i)
            for j in range(2):
                pool.wait_ge(out_stored[j], 16 * PANELS // 2)

        @block.scalar
        def _(act):
            def sum_quarter(g, p, k):
                act.wait_ge(rows_in[k], 16 * (p + 1))
                before = [j for j in range(k) if j not in dve_sums(g)]
                if before:
                    act.wait_ge(summed[before[-1]], p + 1)
                elif not isinstance(p, int) or p > 0:
                    act.wait_ge(summed[QUARTERS - 1], p)
                for r in range(ROWGROUPS):
                    ins = act.activation(unused[:, r, :], raw[:, k, r * QW // ROWGROUPS:(r + 1) * QW // ROWGROUPS],
                                         ACT.Copy, accum_out=sums[:, p % 2, k, r:r + 1])
                ins.then_inc(summed[k], 1)

            def high_part(src, n, slot, distance):
                used = n - distance + 1
                if not isinstance(used, int) or used > 0:
                    act.wait_ge(chunk_used, used)
                act.activation(hi[:, slot, :], src, ACT.Copy).then_inc(hi_done, 1)

            def y_high(p):
                act.wait_ge(dis_done, p + 1)
                act.wait_ge(y_ps_done, p + 1)
                act.activation(y[:, p, 0:D], y_ps[:, 0:D], ACT.Copy, scale=dis[:, bass.ds(p, 1)])\
                    .then_inc(y_hi_done, 1)

            def rows_panel(g, q):
                p, n0 = g * TILES + q, rows_base(g) + q * g
                if not isinstance(p, int) or p > 1:
                    act.wait_ge(row_sum_done, p - 1)
                for k in range(QUARTERS):
                    if k not in dve_sums(g):
                        sum_quarter(g, p, k)
                    for c in range(split_by(g, k - 1), split_by(g, k)):
                        act.wait_ge(transposed, n0 + c + 1)
                        high_part(tr[:, c % 2, :], n0 + c, ring_slot(c, g), distances["rows", g][c])
                    if k == 2 and (not isinstance(p, int) or p > 0):
                        y_high(p - 1)

            for g in range(GROUPS):
                peeled = {0: 2, 1: 1}.get(g, 0)
                for q in range(peeled):
                    rows_panel(g, q)
                with act.Fori(peeled, TILES) as q:
                    rows_panel(g, q)

            def cols_turn(g, i):
                for t in range(TURN):
                    act.wait_ge(cols_in[t], 16 * (g * TILES + i + 1))
                    high_part(raw_chunk(t), cols_base(g) + i * TURN + t, ring_slot(t, TURN),
                              distances["cols", g][t])
                    if (g, t) == (0, 1) and isinstance(i, int):
                        y_high(PANELS - 1)

            cols_turn(0, 0)
            for g in range(GROUPS // 2):
                with act.Fori(1 if g == 0 else 0, TILES) as i:
                    cols_turn(g, i)

        @block.vector
        def _(dve):
            dve.wait_ge(consts_made, 3 + ROWGROUPS)

            def transpose(g, n0, c):
                split = n0 + c - 1 if c >= 2 else n0
                if not isinstance(split, int) or split > 0:
                    dve.wait_ge(lo_done, split)
                k, h = c // 2, c % 2 * TILES
                blocks = raw[:, k, :].rearrange("p (r t c) -> p t r c", r=ROWGROUPS, c=Q)[:, h:h + TILES]
                dve.transpose(tr[:, c % 2, :].rearrange("p (t r c) -> p t r c", t=TILES, c=Q), blocks)\
                    .then_inc(transposed, 1)

            def low_part(src, n, slot):
                dve.wait_ge(hi_done, n + 1)
                dve.tensor_tensor(lo[:, slot, :], src, hi[:, slot, :].bitcast(F32), ALU.subtract)\
                    .then_inc(lo_done, 1)

            def sum_quarter(p, k):
                dve.wait_ge(rows_in[k], 16 * (p + 1))
                dve.tensor_reduce(sums[:, p % 2, k, :], raw[:, k, :].rearrange("p (r c) -> p r c", r=ROWGROUPS),
                                  AX_X, ALU.add).then_inc(summed[k], 1)

            def spread_sums(p):
                for k in range(QUARTERS):
                    dve.wait_ge(summed[k], p + 1)
                dve.tensor_reduce(row_sum[:, :], sums[:, p % 2, :, :].rearrange("p k r -> p r k"), AX_X, ALU.add)\
                    .then_inc(row_sum_done, 1)
                dve.wait_ge(row_sum_done, p + 1)
                if not isinstance(p, int) or p > 0:
                    dve.wait_ge(fold_done, p)
                dve.tensor_tensor(spread[:, :, :], same_row[:, None, :].to_broadcast([P, ROWGROUPS, Q]),
                                  row_sum[:, :, None].to_broadcast([P, ROWGROUPS, Q]), ALU.mult)\
                    .then_inc(spread_done, 1)

            def degrees(p):
                dve.wait_ge(fold_done, p + 1)
                if not isinstance(p, int) or p > 0:
                    dve.wait_ge(dis_done, p)
                dve.tensor_scalar(deg_col[:, :], deg_ps[:, 0:1], DEG_EPS, None, ALU.add).then_inc(deg_done, 1)

            def y_low(p):
                dve.wait_ge(y_hi_done, p + 1)
                dve.scalar_tensor_tensor(out=y[:, p, D:2 * D], in0=y_ps[:, 0:D], scalar=dis[:, bass.ds(p, 1)],
                                         in1=y[:, p, 0:D].bitcast(F32), op0=ALU.mult, op1=ALU.subtract)\
                    .then_inc(y_done, 1)

            def save_partial(p, chunks):
                m = p - TILES
                dve.wait_ge(chunk_used, chunks)
                if not isinstance(m, int) or m > 0:
                    dve.wait_ge(spill_out, 16 * m)
                dve.tensor_copy(spill[:, :], prod[:, p % 2, D:2 * D]).then_inc(half_read, 1)
                dve.wait_ge(half_read, m + 1)
                dve.tensor_tensor(spill[:, :], prod[:, p % 2, 0:D], spill[:, :], ALU.add).then_inc(prod_read, 1)

            def rows_panel(g, q, with_last, with_partial):
                p, n0 = g * TILES + q, rows_base(g) + q * g

                def next_transpose(c):
                    if c % 2 == 0:
                        dve.wait_ge(rows_in[c // 2], 16 * (p + 1))
                    transpose(g, n0, c)

                if g > 0:
                    next_transpose(0)
                for c in range(max(g, 1)):
                    last = c >= g - 1
                    if c + 1 < g:
                        next_transpose(c + 1)
                    if g > 0:
                        low_part(tr[:, c % 2, :], n0 + c, ring_slot(c, g))
                    if with_last and c == SPREAD_AFTER:
                        spread_sums(p - 1)
                    if c == 0 and dve_sums(g):
                        sum_quarter(p, 0)
                    if with_partial and (c == SAVE_AFTER or last and c < SAVE_AFTER):
                        save_partial(p - 1, n0)
                    if with_last and (c == DEGREES_AFTER or last and c < DEGREES_AFTER):
                        degrees(p - 1)
                    if with_last and (c == Y_AFTER or last and c < Y_AFTER):
                        y_low(p - 1)
                    if last and 2 in dve_sums(g):
                        sum_quarter(p, 2)

            for g in range(GROUPS):
                peeled = 2 if g <= 1 else 0
                for q in range(peeled):
                    rows_panel(g, q, with_last=g + q > 0, with_partial=g * q > 0)
                with dve.Fori(peeled, TILES) as q:
                    rows_panel(g, q, with_last=True, with_partial=g > 0)
            spread_sums(PANELS - 1)

            def add_up(g, i, j):
                p, seq = turn_panels(g, i)[j], 2 * (g * TILES + i) + j
                m = FIRST_PANELS + seq
                chunks = cols_base(g) + i * TURN + (CHUNKS - g if j == 0 else TURN)
                ours = part[:, i % 2, j, :]
                dve.wait_ge(chunk_used, chunks)
                dve.wait_ge(res_done, seq + 1)
                if g > 0 or not isinstance(i, int) or i > 0:
                    dve.wait_ge(out_stored[j], 16 * (g * TILES + i))
                if g > 0 or j > 0:
                    dve.tensor_tensor(ours, prod[:, j, D:2 * D], ours, ALU.add).then_inc(half_read, 1)
                else:
                    dve.tensor_copy(ours, prod[:, j, D:2 * D]).then_inc(half_read, 1)
                dve.wait_ge(half_read, m + 1)
                dve.tensor_tensor(ours, prod[:, j, 0:D], ours, ALU.add).then_inc(prod_read, 1)
                dve.wait_ge(prod_read, m + 1)
                dve.scalar_tensor_tensor(out=z[:, j, :], in0=ours, scalar=dis[:, bass.ds(p, 1)],
                                         in1=res[:, i % 2, j, :], op0=ALU.mult, op1=ALU.add).then_inc(z_done, 1)
                wait_apart(dve, z_done, seq + 1)
                dve.bn_stats(stats[:, :], z[:, j, :]).then_inc(stats_done, 1)
                wait_apart(dve, stats_done, seq + 1)
                dve.bn_aggr(mean_var[:, :], stats[:, :]).then_inc(mean_var_done, 1)
                dve.wait_ge(mean_var_done, seq + 1)
                dve.tensor_scalar(var_eps[:, :], mean_var[:, 1:2], NORM_EPS, None, ALU.add).then_inc(var_done, 1)

            def normalise(g, i, j):
                dve.wait_ge(rstd_done, 2 * (g * TILES + i) + j + 1)
                dve.tensor_scalar(z[:, j, :], z[:, j, :], mean_var[:, 0:1], rstd[:, :], ALU.subtract, ALU.mult)\
                    .then_inc(out_done, 1)

            def finish(g, i, t, before):
                for (of_g, of_i), place in ((before, t + TURN), ((g, i), t)):
                    for j in range(2):
                        end = CHUNKS - of_g if j == 0 else TURN
                        if of_i is not None and place == end + 1:
                            add_up(of_g, of_i, j)
                        if of_i is not None and place == end + 2:
                            normalise(of_g, of_i, j)

            def cols_turn(g, i, before):
                for t in range(TURN):
                    low_part(raw_chunk(t), cols_base(g) + i * TURN + t, ring_slot(t, TURN))
                    finish(g, i, t, before)
                    if before[1] is None:
                        if t == 0:
                            degrees(PANELS - 1)
                        if t == 1:
                            save_partial(PANELS - 1, FIRST_CHUNKS)
                        if t == 3:
                            y_low(PANELS - 1)

            for g in range(GROUPS // 2):
                cols_turn(g, 0, (g - 1, TILES - 1) if g > 0 else (0, None))
                if g == 0:
                    cols_turn(0, 1, (0, 0))
                with dve.Fori(2 if g == 0 else 1, TILES) as i:
                    cols_turn(g, i, (g, i - 1))
            for j, step in ((1, add_up), (1, normalise)):
                step(GROUPS // 2 - 1, TILES - 1, j)

        @block.tensor
        def _(pe):
            def fold_sums(p):
                pe.wait_ge(spread_done, p + 1)
                if not isinstance(p, int) or p > 0:
                    pe.wait_ge(deg_done, p)
                pe.matmul(deg_ps[:, 0:1], spread[:, :, :].rearrange("p r c -> p (r c)"), ones[:, :],
                          start=True, stop=True).then_inc(fold_done, 1)

            def x_w(p):
                pe.wait_ge(xt_in, 16 * (p + 1))
                if not isinstance(p, int) or p > 0:
                    pe.wait_ge(y_done, p)
                for h in range(2):
                    ins = pe.matmul(y_ps[:, 0:D], xt_sb[:, h, :], wt_sb[:, h, :], start=h == 0, stop=h == 1)
                ins.then_inc(y_ps_done, 1)

            def multiply(bank, n, slot, c, first, last):
                pe.wait_ge(lo_done, n + 1)
                for t in range(TILES):
                    tile = c * TILES + t
                    cols = slice(t * P, (t + 1) * P)

                    def by_high(stop):
                        return pe.matmul(prod[:, bank, :], hi[:, slot, cols], y[:, tile, :],
                                         start=first and t == 0, stop=stop)

                    def by_low():
                        return pe.matmul(prod[:, bank, D:2 * D], lo[:, slot, cols], y[:, tile, 0:D],
                                         start=False, stop=False)

                    if t < TILES - 1:
                        by_high(False)
                        by_low()
                    else:
                        by_low()
                        by_high(last).then_inc(chunk_used, 1)

            def rows_panel(g, q, with_last):
                p, n0 = g * TILES + q, rows_base(g) + q * g
                m = p - TILES
                if with_last and g <= 1:
                    fold_sums(p - 1)
                    x_w(p - 1)
                if g > 0 and (not isinstance(m, int) or m > 1):
                    pe.wait_ge(prod_read, m - 1)
                for c in range(g):
                    if c == g - 1:
                        pe.wait_ge(y_done, TILES * g)
                    multiply(p % 2, n0 + c, ring_slot(c, g), c, c == 0, c == g - 1)
                    if g > 1 and c == FOLD_AFTER:
                        fold_sums(p - 1)
                        x_w(p - 1)

            pe.wait_ge(const_in, 32)
            for g in range(GROUPS):
                peeled = 2 if g <= 1 else 0
                for q in range(peeled):
                    rows_panel(g, q, with_last=g + q > 0)
                with pe.Fori(peeled, TILES) as q:
                    rows_panel(g, q, with_last=True)
            fold_sums(PANELS - 1)
            x_w(PANELS - 1)

            for g in range(GROUPS // 2):
                with pe.Fori(0, TILES) as i:
                    for t in range(TURN):
                        j, c = turn_chunk(g, t)
                        if t in (0, CHUNKS - g):
                            pe.wait_ge(prod_read, FIRST_PANELS + 2 * (g * TILES + i) + j - 1)
                        if c == CHUNKS - 1:
                            pe.wait_ge(y_done, PANELS)
                        multiply(j, cols_base(g) + i * TURN + t, ring_slot(t, TURN), c,
                                 t in (0, CHUNKS - g), c == CHUNKS - 1)


def kernel(x, adj, L0_gnn_W, L0_gnn_b):
    import numpy as _np
    import concourse.bacc as _bacc
    from concourse import mybir as _mybir
    from concourse.bass_utils import run_bass_kernel_spmd as _run

    x, adj, w, b = (_np.asarray(a) for a in (x, adj, L0_gnn_W, L0_gnn_b))
    arrays = {
        "adj_rows": _np.ascontiguousarray(
            adj.reshape(PANELS, ROWGROUPS, Q, QUARTERS, QT, ROWGROUPS, Q).transpose(0, 3, 5, 2, 1, 4, 6)
        ).reshape(PANELS, QUARTERS, P, QW),
        "adj_cols": _np.ascontiguousarray(
            adj.reshape(PANELS, P, CHUNKS, TILES, P).transpose(0, 2, 4, 3, 1)
        ).reshape(PANELS, CHUNKS, P, CW),
        "x": _np.ascontiguousarray(x),
        "x_t": _np.ascontiguousarray(x.reshape(PANELS, P, 2, P).transpose(0, 3, 2, 1)),
        "w_t": _np.ascontiguousarray(w.reshape(D, 2, P).transpose(2, 1, 0)),
        "bias": _np.ascontiguousarray(_np.broadcast_to(b, (P, D))),
    }
    nc = _bacc.Bacc("TRN2", target_bir_lowering=False, num_devices=1)
    f32 = _mybir.dt.float32
    ins = {k: nc.dram_tensor(k, a.shape, f32, kind="ExternalInput").ap() for k, a in arrays.items()}
    out = nc.dram_tensor("out", (N, D), f32, kind="ExternalOutput").ap()
    partial = nc.dram_tensor("partial", (PANELS, P, D), f32).ap()
    gnn_kernel(nc, out=out, partial=partial, **ins)
    r = _run(nc, [arrays], core_ids=[0])
    return r.results[0]["out"]
```

```python
import concourse.bass as bass
from concourse import mybir
from concourse.alu_op_type import AluOpType as ALU
from contextlib import ExitStack

F32 = mybir.dt.float32
F32R = mybir.dt.float32r
ACT = mybir.ActivationFunctionType
AX_X = mybir.AxisListType.X

P = 128
N = 8192
D = 256
Q = 32
PANELS = N // P
TILES = 8
CHUNKS = PANELS // TILES
GROUPS = CHUNKS
CW = TILES * P
QUARTERS = 4
QW = N // QUARTERS
ROWGROUPS = P // Q
RING = 3
DEG_EPS = 1e-8
NORM_EPS = 1e-5

FIRST_CHUNKS = TILES * sum(range(GROUPS))
FIRST_PANELS = PANELS - TILES
TURN = CHUNKS + 1
FOLD_AFTER = 0
SPREAD_AFTER, SAVE_AFTER, DEGREES_AFTER = 0, 1, 2


def dve_rows(g, k):
    return {0: (4, 4, 4, 4, 2, 1, 0, 0), 2: (4, 4, 4, 0, 0, 0, 0, 0)}.get(k, (0,) * GROUPS)[g]


def sums_before(g, k, idle):
    return TILES * sum(dve_rows(j, k) != idle for j in range(g))


LATE_CHUNKS = (7, 4, 5, 6)


def place_of(c):
    return (c, 0) if c < QUARTERS else (LATE_CHUNKS.index(c), 1)


def rows_order(g):
    return {5: [0, 1, 2, 4, 3], 6: [0, 1, 4, 2, 3, 5], 7: [0, 1, 4, 2, 5, 3, 6]}.get(g, list(range(g)))


def rows_base(g):
    return TILES * sum(range(g))


def cols_base(g):
    return FIRST_CHUNKS + TILES * TURN * g


def ring_slot(t, period):
    return 1 if period > 1 and period % RING == 1 and t == period - 1 else t % RING


def ring_distances():
    periods = [("rows", g, g) for g in range(1, GROUPS)] + [("cols", g, TURN) for g in range(GROUPS // 2)]
    used, n, found = {}, 0, {}
    for sweep, g, period in periods:
        least = [RING] * period
        for _ in range(TILES):
            for t in range(period):
                slot = ring_slot(t, period)
                least[t] = min(least[t], n - used.get(slot, -RING))
                used[slot] = n
                n += 1
        found[sweep, g] = least
    return found


def gnn_kernel(nc, adj_rows, adj_cols, x, x_t, w_t, bias, out, partial):
    x_panels = x.rearrange("(n p) d -> n p d", p=P)
    out_panels = out.rearrange("(n p) d -> n p d", p=P)

    ctx = ExitStack()
    with ctx:
        def sb(name, shape, dt=F32):
            return ctx.enter_context(nc.sbuf_tensor(name, shape, dt))

        def sem(name):
            return ctx.enter_context(nc.semaphore(name))

        raw = sb("raw", [P, QUARTERS, QW])
        tr = sb("tr", [P, 2, CW])
        raw_more = sb("raw_more", [P, CW])
        hi = sb("hi", [P, RING, CW], F32R)
        lo = sb("lo", [P, RING, CW], F32R)
        y = sb("y", [P, PANELS, 2 * D], F32R)
        wt_sb = sb("wt_sb", [P, 2, D])
        xt_sb = sb("xt_sb", [P, 2, P])
        bias_sb = sb("bias_sb", [P, D])
        same_row = sb("same_row", [P, Q])
        minus_half = sb("minus_half", [P, 1])
        ones = sb("ones", [P, 1])
        sums = sb("sums", [P, 2, QUARTERS, ROWGROUPS])
        row_sum = sb("row_sum", [P, ROWGROUPS])
        spread = sb("spread", [P, ROWGROUPS, Q])
        deg_col = sb("deg_col", [P, 1])
        dis = sb("dis", [P, PANELS])
        spill = sb("spill", [P, D])
        res = tr[:, 0, :].rearrange("p (i j d) -> p i j d", i=2, j=2)
        part = tr[:, 1, :].rearrange("p (i j d) -> p i j d", i=2, j=2)
        z = sb("z", [P, 2, D])
        stats = sb("stats", [P, 6])
        mean_var = sb("mean_var", [P, 2])
        var_eps = sb("var_eps", [P, 1])
        rstd = sb("rstd", [P, 1])

        prod = ctx.enter_context(nc.psum_tensor("prod", [P, 2, 2 * D], F32))
        y_ps = ctx.enter_context(nc.psum_tensor("y_ps", [P, 2 * D], F32))
        deg_ps = ctx.enter_context(nc.psum_tensor("deg_ps", [P, 2 * D], F32))
        unused = ctx.enter_context(nc.psum_tensor("unused", [P, ROWGROUPS, QW // ROWGROUPS], F32))

        rows_in = [sem(f"rows_in{k}") for k in range(QUARTERS)]
        cols_in = [sem(f"cols_in{k}") for k in range(TURN)]
        const_in = sem("const_in")
        xt_in = sem("xt_in")
        res_in = sem("res_in")
        consts_made = sem("consts_made")
        act_summed = [sem(f"act_summed{k}") for k in range(QUARTERS)]
        dve_summed = [sem(f"dve_summed{k}") for k in range(QUARTERS)]
        transposed = sem("transposed")
        hi_done = sem("hi_done")
        lo_done = sem("lo_done")
        chunk_used = sem("chunk_used")
        row_sum_done = sem("row_sum_done")
        spread_done = sem("spread_done")
        fold_done = sem("fold_done")
        deg_done = sem("deg_done")
        dis_done = sem("dis_done")
        y_ps_done = sem("y_ps_done")
        y_hi_done = sem("y_hi_done")
        y_done = sem("y_done")
        half_read = sem("half_read")
        prod_read = sem("prod_read")
        spill_out = sem("spill_out")
        res_done = sem("res_done")
        z_done = sem("z_done")
        stats_done = sem("stats_done")
        mean_var_done = sem("mean_var_done")
        var_done = sem("var_done")
        rstd_done = sem("rstd_done")
        out_done = sem("out_done")
        out_stored = [sem(f"out_stored{j}") for j in range(2)]

        block = ctx.enter_context(nc.Block())

        def wait_apart(eng, semaphore, count):
            eng.compute_val(count)
            eng.wait_ge(consts_made, 3 + ROWGROUPS)
            eng.wait_ge(semaphore, count)

        def raw_chunk(slot):
            return raw[:, slot // 2, slot % 2 * CW:(slot % 2 + 1) * CW] if slot < CHUNKS else raw_more[:, :]

        def tr_slot(c, g):
            slot = ring_slot(c, g)
            return tr[:, slot, :] if slot < 2 else raw_more[:, :]

        distances = ring_distances()

        def wait_summed(wait, g, q, k):
            if dve_rows(g, k) < ROWGROUPS:
                wait(act_summed[k], sums_before(g, k, ROWGROUPS) + q + 1)
            if dve_rows(g, k) > 0:
                wait(dve_summed[k], sums_before(g, k, 0) + q + 1)

        def turn_chunk(g, t):
            return (0, g + t) if t < CHUNKS - g else (1, t - 1)

        def turn_panels(g, i):
            return g * TILES + i, (GROUPS - 1 - g) * TILES + i

        def res_loads(g, i):
            return (3 * TILES if g > 0 else 0) + max(g - 1, 0) * 4 * TILES + (4 if g > 0 else 3) * (i + 1)

        @block.sync
        def _(sp):
            def load_quarter(p, k):
                sp.dma_start(raw[:, k, :], adj_rows[p, k, :, :]).then_inc(rows_in[k], 16)

            def wait_quarter_used(g, p, q, k):
                wait_summed(lambda semaphore, count: wait_apart(sp, semaphore, count), g, q, k)
                places = [t for t, c in enumerate(rows_order(g)) if place_of(c)[0] == k]
                if places:
                    wait_apart(sp, transposed, rows_base(g) + q * g + places[-1] + 1)

            for k in range(QUARTERS):
                load_quarter(0, k)
            for g in range(GROUPS):
                last = g == GROUPS - 1
                with sp.Fori(0, TILES - 1 if last else TILES) as q:
                    p = g * TILES + q
                    for k in range(QUARTERS):
                        wait_quarter_used(g, p, q, k)
                        load_quarter(p + 1, k)

            def load_chunk(g, i, t):
                j, c = turn_chunk(g, t)
                sp.dma_start(raw_chunk(t), adj_cols[turn_panels(g, i)[j], c, :, :]).then_inc(cols_in[t], 16)

            def load_res(g, i):
                turn = g * TILES + i
                if not isinstance(turn, int) or turn > 0:
                    wait_apart(sp, res_in, 16 * res_loads(g, i - 1))
                if not isinstance(turn, int) or turn > 1:
                    wait_apart(sp, z_done, 2 * turn - 2)
                for j, p in enumerate(turn_panels(g, i)):
                    sp.dma_start(res[:, i % 2, j, :], x_panels[p, :, :]).then_inc(res_in, 16)
                    if g > 0 or j > 0:
                        sp.dma_start(part[:, i % 2, j, :], partial[p, :, :]).then_inc(res_in, 16)

            for t in range(CHUNKS):
                if t % 2 == 0:
                    wait_quarter_used(GROUPS - 1, PANELS - 1, TILES - 1, t // 2)
                load_chunk(0, 0, t)
            sp.wait_ge(lo_done, FIRST_CHUNKS)
            load_chunk(0, 0, TURN - 1)
            sp.wait_ge(spill_out, 16 * FIRST_PANELS)
            load_res(0, 0)

            def load_turn(g, i):
                for t in range(TURN):
                    wait_apart(sp, lo_done, cols_base(g) + (i - 1) * TURN + t + 1)
                    load_chunk(g, i, t)
                    if t == 2:
                        load_res(g, i)

            load_turn(0, 1)
            for g in range(GROUPS // 2):
                with sp.Fori(2 if g == 0 else 0, TILES) as i:
                    load_turn(g, i)

        @block.gpsimd
        def _(pool):
            pool.dma_start(wt_sb[:, :, :], w_t).then_inc(const_in, 16)
            pool.dma_start(bias_sb[:, :], bias).then_inc(const_in, 16)
            pool.dma_start(xt_sb[:, :, :], x_t[0, :, :, :]).then_inc(xt_in, 16)
            pool.memset(minus_half[:, :], -0.5).then_inc(consts_made, 1)
            pool.memset(ones[:, :], 1.0).then_inc(consts_made, 1)
            pool.memset(same_row[:, :], 0.0).then_inc(consts_made, 1)
            for a in range(ROWGROUPS):
                pool.wait_ge(consts_made, 3 + a)
                pool.affine_select(out=same_row[:, :], in_=same_row[:, :], compare_op=ALU.not_equal, fill=1.0,
                                   base=-Q * a, pattern=[[-1, Q]], channel_multiplier=1).then_inc(consts_made, 1)

            def powers(p):
                wait_apart(pool, deg_done, p + 1)
                pool.tensor_tensor(dis[:, bass.ds(p, 1)], deg_col[:, :], minus_half[:, :], ALU.pow)\
                    .then_inc(dis_done, 1)

            def store_partial(p):
                pool.wait_ge(prod_read, p - TILES + 1)
                pool.dma_start(partial[p, :, :], spill[:, :]).then_inc(spill_out, 16)

            def load_xt(p):
                pool.wait_ge(y_ps_done, p)
                pool.dma_start(xt_sb[:, :, :], x_t[p, :, :, :]).then_inc(xt_in, 16)

            with pool.Fori(1, TILES + 1) as p:
                powers(p - 1)
                load_xt(p)
            with pool.Fori(TILES + 1, PANELS) as p:
                powers(p - 1)
                load_xt(p)
                store_partial(p - 1)
            powers(PANELS - 1)
            store_partial(PANELS - 1)

            def add_bias(g, i):
                wait_apart(pool, res_in, 16 * res_loads(g, i))
                for j in range(2):
                    pool.tensor_tensor(res[:, i % 2, j, :], res[:, i % 2, j, :], bias_sb[:, :], ALU.add)\
                        .then_inc(res_done, 1)

            def finish(g, i):
                for j, p in enumerate(turn_panels(g, i)):
                    done = 2 * (g * TILES + i) + j + 1
                    pool.wait_ge(var_done, done)
                    pool.tensor_tensor(rstd[:, :], var_eps[:, :], minus_half[:, :], ALU.pow).then_inc(rstd_done, 1)
                    pool.wait_ge(out_done, done)
                    pool.dma_start(out_panels[p, :, :], z[:, j, :]).then_inc(out_stored[j], 16)

            for g in range(GROUPS // 2):
                with pool.Fori(0, TILES) as i:
                    add_bias(g, i)
                    finish(g, i)
            for j in range(2):
                pool.wait_ge(out_stored[j], 16 * PANELS // 2)

        @block.scalar
        def _(act):
            def sum_rows(g, q, k, r):
                p = g * TILES + q
                if r == dve_rows(g, k):
                    act.wait_ge(rows_in[k], 16 * (p + 1))
                    before = [j for j in range(k) if dve_rows(g, j) < ROWGROUPS]
                    if before:
                        act.wait_ge(act_summed[before[-1]], sums_before(g, before[-1], ROWGROUPS) + q + 1)
                    elif not isinstance(p, int) or p > 0:
                        act.wait_ge(act_summed[QUARTERS - 1], p)
                ins = act.activation(unused[:, r, :], raw[:, k, r * QW // ROWGROUPS:(r + 1) * QW // ROWGROUPS],
                                     ACT.Copy, accum_out=sums[:, p % 2, k, r:r + 1])
                if r == ROWGROUPS - 1:
                    ins.then_inc(act_summed[k], 1)

            def high_part(src, n, slot, distance):
                used = n - distance + 1
                if not isinstance(used, int) or used > 0:
                    act.wait_ge(chunk_used, used)
                act.activation(hi[:, slot, :], src, ACT.Copy).then_inc(hi_done, 1)

            def y_high(p):
                act.wait_ge(dis_done, p + 1)
                act.wait_ge(y_ps_done, p + 1)
                act.activation(y[:, p, 0:D], y_ps[:, 0:D], ACT.Copy, scale=dis[:, bass.ds(p, 1)])\
                    .then_inc(y_hi_done, 1)

            def rows_panel(g, q):
                p, n0 = g * TILES + q, rows_base(g) + q * g
                if not isinstance(p, int) or p > 1:
                    act.wait_ge(row_sum_done, p - 1)
                ours = [(k, r) for k in range(QUARTERS) for r in range(dve_rows(g, k), ROWGROUPS)]
                c = 0
                for at, (k, r) in enumerate(ours):
                    while c < g and c * len(ours) <= at * g:
                        if g >= QUARTERS and c == g - 1:
                            y_high(p - 1)
                        act.wait_ge(transposed, n0 + c + 1)
                        high_part(tr_slot(c, g), n0 + c, ring_slot(c, g), distances["rows", g][c])
                        c += 1
                    if g < QUARTERS and (k, r) == (QUARTERS - 1, 0) and (not isinstance(p, int) or p > 0):
                        y_high(p - 1)
                    sum_rows(g, q, k, r)

            for g in range(GROUPS):
                peeled = {0: 2, 1: 1}.get(g, 0)
                for q in range(peeled):
                    rows_panel(g, q)
                with act.Fori(peeled, TILES) as q:
                    rows_panel(g, q)

            def cols_turn(g, i):
                for t in range(TURN):
                    act.wait_ge(cols_in[t], 16 * (g * TILES + i + 1))
                    high_part(raw_chunk(t), cols_base(g) + i * TURN + t, ring_slot(t, TURN),
                              distances["cols", g][t])
                    if (g, t) == (0, 1) and isinstance(i, int):
                        y_high(PANELS - 1)

            cols_turn(0, 0)
            for g in range(GROUPS // 2):
                with act.Fori(1 if g == 0 else 0, TILES) as i:
                    cols_turn(g, i)

        @block.vector
        def _(dve):
            dve.wait_ge(consts_made, 3 + ROWGROUPS)

            def transpose(g, p, n, c):
                k, half = place_of(rows_order(g)[c])
                dve.wait_ge(rows_in[k], 16 * (p + 1))
                split = n - 1 if g > 1 and not (g == 2 and isinstance(n, int) and n == rows_base(2)) else n
                if not isinstance(split, int) or split > 0:
                    dve.wait_ge(lo_done, split)
                blocks = raw[:, k, :].rearrange("p (r t c) -> p t r c", r=ROWGROUPS, c=Q)
                blocks = blocks[:, half * TILES:(half + 1) * TILES]
                dve.transpose(tr_slot(c, g).rearrange("p (t r c) -> p t r c", t=TILES, c=Q), blocks)\
                    .then_inc(transposed, 1)

            def low_part(src, n, slot):
                dve.wait_ge(hi_done, n + 1)
                dve.tensor_tensor(lo[:, slot, :], src, hi[:, slot, :].bitcast(F32), ALU.subtract)\
                    .then_inc(lo_done, 1)

            def sum_quarter(g, p, k):
                rows = dve_rows(g, k)
                dve.wait_ge(rows_in[k], 16 * (p + 1))
                dve.tensor_reduce(sums[:, p % 2, k, 0:rows],
                                  raw[:, k, :].rearrange("p (r c) -> p r c", r=ROWGROUPS)[:, 0:rows, :],
                                  AX_X, ALU.add).then_inc(dve_summed[k], 1)

            def spread_sums(g, q):
                p = g * TILES + q
                for k in range(QUARTERS):
                    wait_summed(dve.wait_ge, g, q, k)
                dve.tensor_reduce(row_sum[:, :], sums[:, p % 2, :, :].rearrange("p k r -> p r k"), AX_X, ALU.add)\
                    .then_inc(row_sum_done, 1)
                dve.wait_ge(row_sum_done, p + 1)
                if not isinstance(p, int) or p > 0:
                    dve.wait_ge(fold_done, p)
                dve.tensor_tensor(spread[:, :, :], same_row[:, None, :].to_broadcast([P, ROWGROUPS, Q]),
                                  row_sum[:, :, None].to_broadcast([P, ROWGROUPS, Q]), ALU.mult)\
                    .then_inc(spread_done, 1)

            def degrees(p):
                dve.wait_ge(fold_done, p + 1)
                if not isinstance(p, int) or p > 0:
                    dve.wait_ge(dis_done, p)
                dve.tensor_scalar(deg_col[:, :], deg_ps[:, 0:1], DEG_EPS, None, ALU.add).then_inc(deg_done, 1)

            def y_low(p):
                dve.wait_ge(y_hi_done, p + 1)
                dve.scalar_tensor_tensor(out=y[:, p, D:2 * D], in0=y_ps[:, 0:D], scalar=dis[:, bass.ds(p, 1)],
                                         in1=y[:, p, 0:D].bitcast(F32), op0=ALU.mult, op1=ALU.subtract)\
                    .then_inc(y_done, 1)

            def save_partial(p, chunks):
                m = p - TILES
                dve.wait_ge(chunk_used, chunks)
                if not isinstance(m, int) or m > 0:
                    dve.wait_ge(spill_out, 16 * m)
                dve.tensor_copy(spill[:, :], prod[:, p % 2, D:2 * D]).then_inc(half_read, 1)
                dve.wait_ge(half_read, m + 1)
                dve.tensor_tensor(spill[:, :], prod[:, p % 2, 0:D], spill[:, :], ALU.add).then_inc(prod_read, 1)

            def rows_panel(g, q, with_last, with_partial, next_g):
                p, n0 = g * TILES + q, rows_base(g) + q * g
                before = (g - 1, TILES - 1) if isinstance(q, int) and q == 0 else (g, q - 1)

                early = g >= QUARTERS
                if early and dve_rows(g, 0) > 0:
                    sum_quarter(g, p, 0)
                for c in range(max(g, 1)):
                    last = c >= g - 1
                    if not last:
                        transpose(g, p, n0 + c + 1, c + 1)
                    elif next_g and early:
                        transpose(next_g, p + 1, n0 + g, 0)
                    if g > 0:
                        low_part(tr_slot(c, g), n0 + c, ring_slot(c, g))
                    if with_last and c == SPREAD_AFTER:
                        spread_sums(*before)
                    if c == 0 and not early and dve_rows(g, 0) > 0:
                        sum_quarter(g, p, 0)
                    if with_partial and (c == SAVE_AFTER or last and c < SAVE_AFTER):
                        save_partial(p - 1, n0)
                    if with_last and (c == DEGREES_AFTER or last and c < DEGREES_AFTER):
                        degrees(p - 1)
                if with_last:
                    y_low(p - 1)
                if dve_rows(g, 2) > 0:
                    sum_quarter(g, p, 2)
                if next_g and not early:
                    transpose(next_g, p + 1, n0 + g, 0)

            for g in range(GROUPS):
                peeled = 2 if g <= 1 else 1
                for q in range(peeled):
                    rows_panel(g, q, with_last=g + q > 0, with_partial=g * TILES + q > TILES, next_g=g)
                with dve.Fori(peeled, TILES - 1) as q:
                    rows_panel(g, q, with_last=True, with_partial=g > 0, next_g=g)
                rows_panel(g, TILES - 1, with_last=True, with_partial=g > 0, next_g=(g + 1) % GROUPS)
            spread_sums(GROUPS - 1, TILES - 1)

            def add_up(g, i, j):
                p, seq = turn_panels(g, i)[j], 2 * (g * TILES + i) + j
                m = FIRST_PANELS + seq
                chunks = cols_base(g) + i * TURN + (CHUNKS - g if j == 0 else TURN)
                ours = part[:, i % 2, j, :]
                dve.wait_ge(chunk_used, chunks)
                dve.wait_ge(res_done, seq + 1)
                if g > 0 or not isinstance(i, int) or i > 0:
                    dve.wait_ge(out_stored[j], 16 * (g * TILES + i))
                if g > 0 or j > 0:
                    dve.tensor_tensor(ours, prod[:, j, D:2 * D], ours, ALU.add).then_inc(half_read, 1)
                else:
                    dve.tensor_copy(ours, prod[:, j, D:2 * D]).then_inc(half_read, 1)
                dve.wait_ge(half_read, m + 1)
                dve.tensor_tensor(ours, prod[:, j, 0:D], ours, ALU.add).then_inc(prod_read, 1)
                dve.wait_ge(prod_read, m + 1)
                dve.scalar_tensor_tensor(out=z[:, j, :], in0=ours, scalar=dis[:, bass.ds(p, 1)],
                                         in1=res[:, i % 2, j, :], op0=ALU.mult, op1=ALU.add).then_inc(z_done, 1)
                wait_apart(dve, z_done, seq + 1)
                dve.bn_stats(stats[:, :], z[:, j, :]).then_inc(stats_done, 1)
                wait_apart(dve, stats_done, seq + 1)
                dve.bn_aggr(mean_var[:, :], stats[:, :]).then_inc(mean_var_done, 1)
                dve.wait_ge(mean_var_done, seq + 1)
                dve.tensor_scalar(var_eps[:, :], mean_var[:, 1:2], NORM_EPS, None, ALU.add).then_inc(var_done, 1)

            def normalise(g, i, j):
                dve.wait_ge(rstd_done, 2 * (g * TILES + i) + j + 1)
                dve.tensor_scalar(z[:, j, :], z[:, j, :], mean_var[:, 0:1], rstd[:, :], ALU.subtract, ALU.mult)\
                    .then_inc(out_done, 1)

            def finish(g, i, t, before):
                for (of_g, of_i), place in ((before, t + TURN), ((g, i), t)):
                    for j in range(2):
                        end = CHUNKS - of_g if j == 0 else TURN
                        if of_i is not None and place == end + 1 + j:
                            add_up(of_g, of_i, j)
                        if of_i is not None and place == end + 2 + j:
                            normalise(of_g, of_i, j)

            def cols_turn(g, i, before):
                for t in range(TURN):
                    low_part(raw_chunk(t), cols_base(g) + i * TURN + t, ring_slot(t, TURN))
                    finish(g, i, t, before)
                    if before[1] is None:
                        if t == 0:
                            degrees(PANELS - 1)
                        if t == 1:
                            save_partial(PANELS - 1, FIRST_CHUNKS)
                        if t == 3:
                            y_low(PANELS - 1)

            for g in range(GROUPS // 2):
                cols_turn(g, 0, (g - 1, TILES - 1) if g > 0 else (0, None))
                if g == 0:
                    cols_turn(0, 1, (0, 0))
                with dve.Fori(2 if g == 0 else 1, TILES) as i:
                    cols_turn(g, i, (g, i - 1))
            for j, step in ((1, add_up), (1, normalise)):
                step(GROUPS // 2 - 1, TILES - 1, j)

        @block.tensor
        def _(pe):
            def fold_sums(p):
                pe.wait_ge(spread_done, p + 1)
                if not isinstance(p, int) or p > 0:
                    pe.wait_ge(deg_done, p)
                pe.matmul(deg_ps[:, 0:1], spread[:, :, :].rearrange("p r c -> p (r c)"), ones[:, :],
                          start=True, stop=True).then_inc(fold_done, 1)

            def x_w(p):
                pe.wait_ge(xt_in, 16 * (p + 1))
                if not isinstance(p, int) or p > 0:
                    pe.wait_ge(y_done, p)
                for h in range(2):
                    ins = pe.matmul(y_ps[:, 0:D], xt_sb[:, h, :], wt_sb[:, h, :], start=h == 0, stop=h == 1)
                ins.then_inc(y_ps_done, 1)

            def multiply(bank, n, slot, c, first, last):
                pe.wait_ge(lo_done, n + 1)
                for t in range(TILES):
                    tile = c * TILES + t
                    cols = slice(t * P, (t + 1) * P)

                    def by_high(stop):
                        return pe.matmul(prod[:, bank, :], hi[:, slot, cols], y[:, tile, :],
                                         start=first and t == 0, stop=stop)

                    def by_low():
                        return pe.matmul(prod[:, bank, D:2 * D], lo[:, slot, cols], y[:, tile, 0:D],
                                         start=False, stop=False)

                    if t < TILES - 1:
                        by_high(False)
                        by_low()
                    else:
                        by_low()
                        by_high(last).then_inc(chunk_used, 1)

            def rows_panel(g, q, with_last):
                p, n0 = g * TILES + q, rows_base(g) + q * g
                m = p - TILES
                if with_last and g <= 1:
                    fold_sums(p - 1)
                    x_w(p - 1)
                if g > 0 and (not isinstance(m, int) or m > 1):
                    pe.wait_ge(prod_read, m - 1)
                for t, c in enumerate(rows_order(g)):
                    if c == g - 1:
                        pe.wait_ge(y_done, TILES * g)
                    multiply(p % 2, n0 + t, ring_slot(t, g), c, t == 0, t == g - 1)
                    if g > 1 and t == FOLD_AFTER:
                        fold_sums(p - 1)
                        x_w(p - 1)

            pe.wait_ge(const_in, 32)
            for g in range(GROUPS):
                peeled = 2 if g <= 1 else 0
                for q in range(peeled):
                    rows_panel(g, q, with_last=g + q > 0)
                with pe.Fori(peeled, TILES) as q:
                    rows_panel(g, q, with_last=True)
            fold_sums(PANELS - 1)
            x_w(PANELS - 1)

            for g in range(GROUPS // 2):
                with pe.Fori(0, TILES) as i:
                    for t in range(TURN):
                        j, c = turn_chunk(g, t)
                        if t in (0, CHUNKS - g):
                            pe.wait_ge(prod_read, FIRST_PANELS + 2 * (g * TILES + i) + j - 1)
                        if c == CHUNKS - 1:
                            pe.wait_ge(y_done, PANELS)
                        multiply(j, cols_base(g) + i * TURN + t, ring_slot(t, TURN), c,
                                 t in (0, CHUNKS - g), c == CHUNKS - 1)


def kernel(x, adj, L0_gnn_W, L0_gnn_b):
    import numpy as _np
    import concourse.bacc as _bacc
    from concourse import mybir as _mybir
    from concourse.bass_utils import run_bass_kernel_spmd as _run

    x, adj, w, b = (_np.asarray(a) for a in (x, adj, L0_gnn_W, L0_gnn_b))
    arrays = {
        "adj_rows": _np.ascontiguousarray(_np.stack([
            adj.reshape(PANELS, ROWGROUPS, Q, CHUNKS, TILES, ROWGROUPS, Q)[:, :, :, chunks]
            for chunks in (list(range(QUARTERS)), list(LATE_CHUNKS))
        ]).transpose(1, 4, 6, 3, 2, 0, 5, 7)).reshape(PANELS, QUARTERS, P, QW),
        "adj_cols": _np.ascontiguousarray(
            adj.reshape(PANELS, P, CHUNKS, TILES, P).transpose(0, 2, 4, 3, 1)
        ).reshape(PANELS, CHUNKS, P, CW),
        "x": _np.ascontiguousarray(x),
        "x_t": _np.ascontiguousarray(x.reshape(PANELS, P, 2, P).transpose(0, 3, 2, 1)),
        "w_t": _np.ascontiguousarray(w.reshape(D, 2, P).transpose(2, 1, 0)),
        "bias": _np.ascontiguousarray(_np.broadcast_to(b, (P, D))),
    }
    nc = _bacc.Bacc("TRN2", target_bir_lowering=False, num_devices=1)
    f32 = _mybir.dt.float32
    ins = {k: nc.dram_tensor(k, a.shape, f32, kind="ExternalInput").ap() for k, a in arrays.items()}
    out = nc.dram_tensor("out", (N, D), f32, kind="ExternalOutput").ap()
    partial = nc.dram_tensor("partial", (PANELS, P, D), f32).ap()
    gnn_kernel(nc, out=out, partial=partial, **ins)
    r = _run(nc, [arrays], core_ids=[0])
    return r.results[0]["out"]
```

```python
import concourse.bass as bass
from concourse import mybir
from concourse.alu_op_type import AluOpType as ALU
from contextlib import ExitStack

F32 = mybir.dt.float32
F32R = mybir.dt.float32r
ACT = mybir.ActivationFunctionType
AX_X = mybir.AxisListType.X

P = 128
N = 8192
D = 256
Q = 32
PANELS = N // P
TILES = 8
CHUNKS = PANELS // TILES
GROUPS = CHUNKS
CW = TILES * P
QUARTERS = 4
QW = N // QUARTERS
ROWGROUPS = P // Q
RING = 3
DEG_EPS = 1e-8
NORM_EPS = 1e-5

FIRST_PANELS = PANELS - TILES
DIAGONALS = PANELS // 2
TURN = CHUNKS
FOLD_AFTER = 0
SPREAD_AFTER, SAVE_AFTER = 0, 1


def dve_rows(g, k):
    return {0: (4, 4, 4, 4, 2, 1, 0, 0), 2: (4, 4, 4, 0, 0, 0, 0, 0)}.get(k, (0,) * GROUPS)[g]


def sums_before(g, k, idle):
    return TILES * sum(dve_rows(j, k) != idle for j in range(g))


LATE_CHUNKS = (7, 4, 5, 6)


def place_of(c):
    return (c, 0) if c < QUARTERS else (LATE_CHUNKS.index(c), 1)


def rows_order(g):
    return {5: [0, 1, 2, 4, 3], 6: [0, 1, 4, 2, 3, 5], 7: [0, 1, 4, 2, 5, 3, 6]}.get(g, list(range(g)))


def y_places(g, q):
    urgent = isinstance(q, int) and q == 0 and g >= QUARTERS
    return (1, g - 2) if urgent else (min(2, max(g - 1, 0)), max(g - 1, 0))


def with_diagonal(g):
    return 1 <= g <= DIAGONALS // TILES


def rows_chunks(g):
    return g + with_diagonal(g)


def rows_base(g):
    return TILES * sum(rows_chunks(j) for j in range(g))


def transposes_base(g):
    return TILES * sum(range(g))


FIRST_CHUNKS = rows_base(GROUPS)


def cols_base(g):
    return FIRST_CHUNKS + TILES * TURN * g


def first_part(g):
    return CHUNKS - 1 - g


def ring_slot(t, period):
    return 1 if period > 1 and period % RING == 1 and t == period - 1 else t % RING


def rows_slot(c, g):
    period = rows_chunks(g)
    return ring_slot((c + period - 2) % period if g == QUARTERS else c, period)


def cols_slot(t):
    return ring_slot((t + TURN - 3) % TURN, TURN)


def ring_distances():
    periods = [("rows", g, rows_chunks(g)) for g in range(1, GROUPS)] + \
        [("cols", g, TURN) for g in range(GROUPS // 2)]
    used, n, found = {}, 0, {}
    for sweep, g, period in periods:
        for q in range(TILES):
            least = found.setdefault((sweep, g, q == 0), [RING] * period)
            for t in range(period):
                slot = rows_slot(t, g) if sweep == "rows" else cols_slot(t)
                least[t] = min(least[t], n - used.get(slot, -RING))
                used[slot] = n
                n += 1
    return found


def gnn_kernel(nc, adj_rows, adj_cols, x, x_t, w_t, bias, out, partial, diagonal):
    x_panels = x.rearrange("(n p) d -> n p d", p=P)
    out_panels = out.rearrange("(n p) d -> n p d", p=P)

    ctx = ExitStack()
    with ctx:
        def sb(name, shape, dt=F32):
            return ctx.enter_context(nc.sbuf_tensor(name, shape, dt))

        def sem(name):
            return ctx.enter_context(nc.semaphore(name))

        raw = sb("raw", [P, QUARTERS, QW])
        tr = sb("tr", [P, 3, CW])
        raw_diagonal = tr[:, 2, :]
        hi = sb("hi", [P, RING, CW], F32R)
        lo = sb("lo", [P, RING, CW], F32R)
        y = sb("y", [P, PANELS, 2 * D], F32R)
        wt_sb = sb("wt_sb", [P, 2, D])
        xt_sb = sb("xt_sb", [P, 2, P])
        bias_sb = sb("bias_sb", [P, D])
        same_row = sb("same_row", [P, Q])
        minus_half = sb("minus_half", [P, 1])
        ones = sb("ones", [P, 1])
        sums = sb("sums", [P, 2, QUARTERS, ROWGROUPS])
        row_sum = sb("row_sum", [P, ROWGROUPS])
        spread = sb("spread", [P, ROWGROUPS, Q])
        deg_col = sb("deg_col", [P, 1])
        dis = sb("dis", [P, PANELS])
        spill = sb("spill", [P, D])
        res = tr[:, 0, :].rearrange("p (i j d) -> p i j d", i=2, j=2)
        part = tr[:, 1, :].rearrange("p (i j d) -> p i j d", i=2, j=2)
        part_more = tr[:, 2, 0:2 * D].rearrange("p (i d) -> p i d", i=2)
        z = sb("z", [P, 2, D])
        spill_diagonal = z[:, 0, :]
        stats = sb("stats", [P, 6])
        mean_var = sb("mean_var", [P, 2])
        var_eps = sb("var_eps", [P, 1])
        rstd = sb("rstd", [P, 1])

        prod = ctx.enter_context(nc.psum_tensor("prod", [P, 3, 2 * D], F32))
        y_ps = ctx.enter_context(nc.psum_tensor("y_ps", [P, 2 * D], F32))
        deg_ps = ctx.enter_context(nc.psum_tensor("deg_ps", [P, 2 * D], F32))
        unused_ps = ctx.enter_context(nc.psum_tensor("unused_ps", [P, ROWGROUPS - 1, QW // ROWGROUPS], F32))
        unused_sb = sb("unused_sb", [P, QW // ROWGROUPS])
        unused = [unused_ps[:, r, :] for r in range(ROWGROUPS - 1)] + [unused_sb[:, :]]

        rows_in = [sem(f"rows_in{k}") for k in range(QUARTERS)]
        cols_in = [sem(f"cols_in{k}") for k in range(TURN)]
        const_in = sem("const_in")
        diagonal_in = sem("diagonal_in")
        xt_in = sem("xt_in")
        res_in = sem("res_in")
        consts_made = sem("consts_made")
        act_summed = [sem(f"act_summed{k}") for k in range(QUARTERS)]
        dve_summed = [sem(f"dve_summed{k}") for k in range(QUARTERS)]
        transposed = sem("transposed")
        hi_done = sem("hi_done")
        lo_done = sem("lo_done")
        chunk_used = sem("chunk_used")
        row_sum_done = sem("row_sum_done")
        spread_done = sem("spread_done")
        fold_done = sem("fold_done")
        deg_done = sem("deg_done")
        dis_done = sem("dis_done")
        y_ps_done = sem("y_ps_done")
        y_hi_done = sem("y_hi_done")
        y_done = sem("y_done")
        half_read = sem("half_read")
        prod_read = sem("prod_read")
        spill_out = sem("spill_out")
        diagonal_half_read = sem("diagonal_half_read")
        diagonal_read = sem("diagonal_read")
        diagonal_out = sem("diagonal_out")
        parts_done = sem("parts_done")
        res_done = sem("res_done")
        z_done = sem("z_done")
        stats_done = sem("stats_done")
        mean_var_done = sem("mean_var_done")
        var_done = sem("var_done")
        rstd_done = sem("rstd_done")
        out_done = sem("out_done")
        out_stored = [sem(f"out_stored{j}") for j in range(2)]

        block = ctx.enter_context(nc.Block())

        def wait_apart(eng, semaphore, count):
            eng.compute_val(count)
            eng.wait_ge(consts_made, 3 + ROWGROUPS)
            eng.wait_ge(semaphore, count)

        def raw_chunk(slot):
            return raw[:, slot // 2, slot % 2 * CW:(slot % 2 + 1) * CW]

        def rows_source(g, c):
            if c == g:
                return raw_diagonal
            return tr[:, c % 2 if with_diagonal(g) else rows_slot(c, g), :]

        distances = ring_distances()

        def wait_summed(wait, g, q, k):
            if dve_rows(g, k) < ROWGROUPS:
                wait(act_summed[k], sums_before(g, k, ROWGROUPS) + q + 1)
            if dve_rows(g, k) > 0:
                wait(dve_summed[k], sums_before(g, k, 0) + q + 1)

        def turn_chunk(g, t):
            return (0, g + 1 + t) if t < first_part(g) else (1, t)

        def turn_panels(g, i):
            return g * TILES + i, (GROUPS - 1 - g) * TILES + i

        def res_loads(g, i):
            return (4 * TILES if g > 0 else 0) + max(g - 1, 0) * 5 * TILES + (5 if g > 0 else 4) * (i + 1)

        @block.sync
        def _(sp):
            def load_quarter(p, k):
                sp.dma_start(raw[:, k, :], adj_rows[p, k, :, :]).then_inc(rows_in[k], 16)

            def wait_quarter_used(g, p, q, k):
                wait_summed(lambda semaphore, count: wait_apart(sp, semaphore, count), g, q, k)
                places = [t for t, c in enumerate(rows_order(g)) if place_of(c)[0] == k]
                if places:
                    wait_apart(sp, transposed, transposes_base(g) + q * g + places[-1] + 1)

            for k in range(QUARTERS):
                load_quarter(0, k)

            def rows_loads(g, q, next_g):
                p = g * TILES + q
                for k in range(QUARTERS):
                    wait_quarter_used(g, p, q, k)
                    load_quarter(p + 1, k)
                if with_diagonal(next_g):
                    if with_diagonal(g):
                        wait_apart(sp, lo_done, rows_base(g) + (q + 1) * rows_chunks(g))
                    sp.dma_start(raw_diagonal, adj_cols[p + 1 - TILES, next_g - 1, :, :])\
                        .then_inc(diagonal_in, 16)

            for g in range(GROUPS):
                with sp.Fori(0, TILES - 1) as q:
                    rows_loads(g, q, g)
                if g < GROUPS - 1:
                    rows_loads(g, TILES - 1, g + 1)

            def load_chunk(g, i, t):
                j, c = turn_chunk(g, t)
                sp.dma_start(raw_chunk(t), adj_cols[turn_panels(g, i)[j], c, :, :]).then_inc(cols_in[t], 16)

            def load_res(g, i):
                turn = g * TILES + i
                if not isinstance(turn, int) or turn > 0:
                    wait_apart(sp, res_in, 16 * res_loads(g, i - 1))
                if not isinstance(turn, int) or turn > 1:
                    wait_apart(sp, z_done, 2 * turn - 2)
                for j, p in enumerate(turn_panels(g, i)):
                    sp.dma_start(res[:, i % 2, j, :], x_panels[p, :, :]).then_inc(res_in, 16)
                    source = partial if g > 0 or j > 0 else diagonal
                    sp.dma_start(part[:, i % 2, j, :], source[p, :, :]).then_inc(res_in, 16)
                    if g > 0 and j == 0:
                        sp.dma_start(part_more[:, i % 2, :], diagonal[p, :, :]).then_inc(res_in, 16)

            for t in range(CHUNKS):
                if t % 2 == 0:
                    wait_quarter_used(GROUPS - 1, PANELS - 1, TILES - 1, t // 2)
                load_chunk(0, 0, t)
            sp.wait_ge(lo_done, FIRST_CHUNKS)
            sp.wait_ge(spill_out, 16 * FIRST_PANELS)
            sp.wait_ge(diagonal_out, 16 * DIAGONALS)
            load_res(0, 0)

            def load_turn(g, i):
                for t in range(TURN):
                    wait_apart(sp, lo_done, cols_base(g) + (i - 1) * TURN + t + 1)
                    load_chunk(g, i, t)
                    if t == 2:
                        load_res(g, i)

            load_turn(0, 1)
            for g in range(GROUPS // 2):
                with sp.Fori(2 if g == 0 else 0, TILES) as i:
                    load_turn(g, i)

        @block.gpsimd
        def _(pool):
            pool.dma_start(wt_sb[:, :, :], w_t).then_inc(const_in, 16)
            pool.dma_start(bias_sb[:, :], bias).then_inc(const_in, 16)
            pool.dma_start(xt_sb[:, :, :], x_t[0, :, :, :]).then_inc(xt_in, 16)
            pool.memset(minus_half[:, :], -0.5).then_inc(consts_made, 1)
            pool.memset(ones[:, :], 1.0).then_inc(consts_made, 1)
            pool.memset(same_row[:, :], 0.0).then_inc(consts_made, 1)
            for a in range(ROWGROUPS):
                pool.wait_ge(consts_made, 3 + a)
                pool.affine_select(out=same_row[:, :], in_=same_row[:, :], compare_op=ALU.not_equal, fill=1.0,
                                   base=-Q * a, pattern=[[-1, Q]], channel_multiplier=1).then_inc(consts_made, 1)

            def powers(p):
                wait_apart(pool, deg_done, p + 1)
                pool.tensor_tensor(dis[:, bass.ds(p, 1)], deg_col[:, :], minus_half[:, :], ALU.pow)\
                    .then_inc(dis_done, 1)

            def store_partial(p):
                pool.wait_ge(prod_read, p - TILES + 1)
                pool.dma_start(partial[p, :, :], spill[:, :]).then_inc(spill_out, 16)

            def store_diagonal(p):
                pool.wait_ge(diagonal_read, p + 1)
                pool.dma_start(diagonal[p, :, :], spill_diagonal).then_inc(diagonal_out, 16)

            def load_xt(p):
                pool.wait_ge(y_ps_done, p)
                pool.dma_start(xt_sb[:, :, :], x_t[p, :, :, :]).then_inc(xt_in, 16)

            with pool.Fori(1, TILES + 1) as p:
                powers(p - 1)
                load_xt(p)
            with pool.Fori(TILES + 1, TILES + 1 + DIAGONALS) as p:
                powers(p - 1)
                load_xt(p)
                store_partial(p - 1)
                store_diagonal(p - 1 - TILES)
            with pool.Fori(TILES + 1 + DIAGONALS, PANELS) as p:
                powers(p - 1)
                load_xt(p)
                store_partial(p - 1)
            powers(PANELS - 1)
            store_partial(PANELS - 1)

            def add_bias(g, i):
                wait_apart(pool, res_in, 16 * res_loads(g, i))
                if g > 0:
                    pool.tensor_tensor(part[:, i % 2, 0, :], part[:, i % 2, 0, :], part_more[:, i % 2, :], ALU.add)\
                        .then_inc(parts_done, 1)
                for j in range(2):
                    pool.tensor_tensor(res[:, i % 2, j, :], res[:, i % 2, j, :], bias_sb[:, :], ALU.add)\
                        .then_inc(res_done, 1)

            def finish(g, i):
                for j, p in enumerate(turn_panels(g, i)):
                    done = 2 * (g * TILES + i) + j + 1
                    pool.wait_ge(var_done, done)
                    pool.tensor_tensor(rstd[:, :], var_eps[:, :], minus_half[:, :], ALU.pow).then_inc(rstd_done, 1)
                    pool.wait_ge(out_done, done)
                    pool.dma_start(out_panels[p, :, :], z[:, j, :]).then_inc(out_stored[j], 16)

            for g in range(GROUPS // 2):
                with pool.Fori(0, TILES) as i:
                    add_bias(g, i)
                    finish(g, i)
            for j in range(2):
                pool.wait_ge(out_stored[j], 16 * PANELS // 2)

        @block.scalar
        def _(act):
            def sum_rows(g, q, k, r):
                p = g * TILES + q
                if r == dve_rows(g, k):
                    act.wait_ge(rows_in[k], 16 * (p + 1))
                    before = [j for j in range(k) if dve_rows(g, j) < ROWGROUPS]
                    if before:
                        act.wait_ge(act_summed[before[-1]], sums_before(g, before[-1], ROWGROUPS) + q + 1)
                    elif not isinstance(p, int) or p > 0:
                        act.wait_ge(act_summed[QUARTERS - 1], p)
                ins = act.activation(unused[r], raw[:, k, r * QW // ROWGROUPS:(r + 1) * QW // ROWGROUPS],
                                     ACT.Copy, accum_out=sums[:, p % 2, k, r:r + 1])
                if r == ROWGROUPS - 1:
                    ins.then_inc(act_summed[k], 1)

            def high_part(src, n, slot, distance):
                used = n - distance + 1
                if not isinstance(used, int) or used > 0:
                    act.wait_ge(chunk_used, used)
                act.activation(hi[:, slot, :], src, ACT.Copy).then_inc(hi_done, 1)

            def y_high(p):
                act.wait_ge(dis_done, p + 1)
                act.wait_ge(y_ps_done, p + 1)
                act.activation(y[:, p, 0:D], y_ps[:, 0:D], ACT.Copy, scale=dis[:, bass.ds(p, 1)])\
                    .then_inc(y_hi_done, 1)

            def rows_panel(g, q):
                p, n0 = g * TILES + q, rows_base(g) + q * rows_chunks(g)
                if not isinstance(p, int) or p > 1:
                    act.wait_ge(row_sum_done, p - 1)

                def rows_high(c):
                    if c < g:
                        act.wait_ge(transposed, transposes_base(g) + q * g + c + 1)
                    else:
                        act.wait_ge(diagonal_in, 16 * (p - TILES + 1))
                    high_part(rows_source(g, c), n0 + c, rows_slot(c, g),
                              distances["rows", g, isinstance(q, int) and q == 0][c])

                ours = [(k, r) for k in range(QUARTERS) for r in range(dve_rows(g, k), ROWGROUPS)]
                c = 0
                for at, (k, r) in enumerate(ours):
                    while c < g and c * len(ours) <= at * g:
                        if g >= QUARTERS and c == y_places(g, q)[1]:
                            y_high(p - 1)
                        rows_high(c)
                        c += 1
                    sum_rows(g, q, k, r)
                if with_diagonal(g):
                    rows_high(g)
                if g < QUARTERS and (not isinstance(p, int) or p > 0):
                    y_high(p - 1)

            for g in range(GROUPS):
                peeled = 2 if g == 0 else 1
                for q in range(peeled):
                    rows_panel(g, q)
                with act.Fori(peeled, TILES) as q:
                    rows_panel(g, q)

            def cols_turn(g, i):
                for t in range(TURN):
                    act.wait_ge(cols_in[t], 16 * (g * TILES + i + 1))
                    high_part(raw_chunk(t), cols_base(g) + i * TURN + t, cols_slot(t),
                              distances["cols", g, isinstance(i, int) and i == 0][t])
                    if (g, t) == (0, 1) and isinstance(i, int):
                        y_high(PANELS - 1)

            for g in range(GROUPS // 2):
                cols_turn(g, 0)
                with act.Fori(1, TILES) as i:
                    cols_turn(g, i)

        @block.vector
        def _(dve):
            dve.wait_ge(consts_made, 3 + ROWGROUPS)

            def transpose(g, p, c, split):
                k, half = place_of(rows_order(g)[c])
                dve.wait_ge(rows_in[k], 16 * (p + 1))
                if not isinstance(split, int) or split > 0:
                    dve.wait_ge(lo_done, split)
                blocks = raw[:, k, :].rearrange("p (r t c) -> p t r c", r=ROWGROUPS, c=Q)
                blocks = blocks[:, half * TILES:(half + 1) * TILES]
                dve.transpose(rows_source(g, c).rearrange("p (t r c) -> p t r c", t=TILES, c=Q), blocks)\
                    .then_inc(transposed, 1)

            def low_part(src, n, slot):
                dve.wait_ge(hi_done, n + 1)
                dve.tensor_tensor(lo[:, slot, :], src, hi[:, slot, :].bitcast(F32), ALU.subtract)\
                    .then_inc(lo_done, 1)

            def sum_quarter(g, p, k):
                rows = dve_rows(g, k)
                dve.wait_ge(rows_in[k], 16 * (p + 1))
                dve.tensor_reduce(sums[:, p % 2, k, 0:rows],
                                  raw[:, k, :].rearrange("p (r c) -> p r c", r=ROWGROUPS)[:, 0:rows, :],
                                  AX_X, ALU.add).then_inc(dve_summed[k], 1)

            def spread_sums(g, q):
                p = g * TILES + q
                for k in range(QUARTERS):
                    wait_summed(dve.wait_ge, g, q, k)
                dve.tensor_reduce(row_sum[:, :], sums[:, p % 2, :, :].rearrange("p k r -> p r k"), AX_X, ALU.add)\
                    .then_inc(row_sum_done, 1)
                dve.wait_ge(row_sum_done, p + 1)
                if not isinstance(p, int) or p > 0:
                    dve.wait_ge(fold_done, p)
                dve.tensor_tensor(spread[:, :, :], same_row[:, None, :].to_broadcast([P, ROWGROUPS, Q]),
                                  row_sum[:, :, None].to_broadcast([P, ROWGROUPS, Q]), ALU.mult)\
                    .then_inc(spread_done, 1)

            def degrees(p):
                dve.wait_ge(fold_done, p + 1)
                if not isinstance(p, int) or p > 0:
                    dve.wait_ge(dis_done, p)
                dve.tensor_scalar(deg_col[:, :], deg_ps[:, 0:1], DEG_EPS, None, ALU.add).then_inc(deg_done, 1)

            def y_low(p):
                dve.wait_ge(y_hi_done, p + 1)
                dve.scalar_tensor_tensor(out=y[:, p, D:2 * D], in0=y_ps[:, 0:D], scalar=dis[:, bass.ds(p, 1)],
                                         in1=y[:, p, 0:D].bitcast(F32), op0=ALU.mult, op1=ALU.subtract)\
                    .then_inc(y_done, 1)

            def save_partial(p, chunks):
                m = p - TILES
                dve.wait_ge(chunk_used, chunks)
                if not isinstance(m, int) or m > 0:
                    dve.wait_ge(spill_out, 16 * m)
                dve.tensor_copy(spill[:, :], prod[:, p % 2, D:2 * D]).then_inc(half_read, 1)
                dve.wait_ge(half_read, m + 1)
                dve.tensor_tensor(spill[:, :], prod[:, p % 2, 0:D], spill[:, :], ALU.add).then_inc(prod_read, 1)

            def save_diagonal(p, chunks):
                dve.wait_ge(chunk_used, chunks)
                if not isinstance(p, int) or p > 0:
                    dve.wait_ge(diagonal_out, 16 * p)
                dve.tensor_copy(spill_diagonal, prod[:, 2, D:2 * D]).then_inc(diagonal_half_read, 1)
                dve.wait_ge(diagonal_half_read, p + 1)
                dve.tensor_tensor(spill_diagonal, prod[:, 2, 0:D], spill_diagonal, ALU.add)\
                    .then_inc(diagonal_read, 1)

            def rows_panel(g, q, with_last, with_partial, next_g):
                p, n0 = g * TILES + q, rows_base(g) + q * rows_chunks(g)
                before = (g - 1, TILES - 1) if isinstance(q, int) and q == 0 else (g, q - 1)

                def low(c):
                    low_part(rows_source(g, c), n0 + c, rows_slot(c, g))

                def rest_of_last():
                    if with_last:
                        y_low(p - 1)
                    if with_partial and with_diagonal(before[0]):
                        save_diagonal(p - 1 - TILES, n0)

                def begin_next(split):
                    if next_g:
                        transpose(next_g, p + 1, 0, split)
                    if early and next_g is not None and dve_rows(next_g, 0) > 0:
                        sum_quarter(next_g, p + 1, 0)

                early = g >= QUARTERS
                for c in range(max(g, 1)):
                    last = c >= g - 1
                    if not last:
                        transpose(g, p, c + 1, n0 + c)
                    elif early:
                        begin_next(n0 + c)
                    if g > 0:
                        low(c)
                    if with_last and c == SPREAD_AFTER:
                        spread_sums(*before)
                    if c == 0 and g <= QUARTERS and (not early or isinstance(q, int) and q == 0):
                        sum_quarter(g, p, 0)
                    if with_partial and (c == SAVE_AFTER or last and c < SAVE_AFTER):
                        save_partial(p - 1, n0)
                    if with_last and c == y_places(g, q)[0]:
                        degrees(p - 1)
                    if early and c == y_places(g, q)[1]:
                        rest_of_last()
                if dve_rows(g, 2) > 0:
                    sum_quarter(g, p, 2)
                in_between = g == QUARTERS - 1 and not (isinstance(q, int) and q == 0)
                if in_between:
                    begin_next(n0 + g)
                if with_diagonal(g):
                    low(g)
                if not early:
                    rest_of_last()
                if not early and not in_between:
                    begin_next(n0 + rows_chunks(g))

            for g in range(GROUPS):
                peeled = 2 if g <= 1 else 1
                for q in range(peeled):
                    rows_panel(g, q, with_last=g + q > 0, with_partial=g * TILES + q > TILES, next_g=g)
                with dve.Fori(peeled, TILES - 1) as q:
                    rows_panel(g, q, with_last=True, with_partial=g > 0, next_g=g)
                rows_panel(g, TILES - 1, with_last=True, with_partial=g > 0,
                           next_g=g + 1 if g < GROUPS - 1 else None)
            spread_sums(GROUPS - 1, TILES - 1)

            def add_up(g, i, j):
                p, seq = turn_panels(g, i)[j], 2 * (g * TILES + i) + j
                m = FIRST_PANELS + seq
                chunks = cols_base(g) + i * TURN + (first_part(g) if j == 0 else TURN)
                ours = part[:, i % 2, j, :]
                dve.wait_ge(chunk_used, chunks)
                dve.wait_ge(res_done, seq + 1)
                if g > 0 or not isinstance(i, int) or i > 0:
                    dve.wait_ge(out_stored[j], 16 * (g * TILES + i))
                if g > 0 and j == 0:
                    dve.wait_ge(parts_done, (g - 1) * TILES + i + 1)
                dve.tensor_tensor(ours, prod[:, j, D:2 * D], ours, ALU.add).then_inc(half_read, 1)
                dve.wait_ge(half_read, m + 1)
                dve.tensor_tensor(ours, prod[:, j, 0:D], ours, ALU.add).then_inc(prod_read, 1)
                dve.wait_ge(prod_read, m + 1)
                dve.scalar_tensor_tensor(out=z[:, j, :], in0=ours, scalar=dis[:, bass.ds(p, 1)],
                                         in1=res[:, i % 2, j, :], op0=ALU.mult, op1=ALU.add).then_inc(z_done, 1)
                wait_apart(dve, z_done, seq + 1)
                dve.bn_stats(stats[:, :], z[:, j, :]).then_inc(stats_done, 1)
                wait_apart(dve, stats_done, seq + 1)
                dve.bn_aggr(mean_var[:, :], stats[:, :]).then_inc(mean_var_done, 1)
                dve.wait_ge(mean_var_done, seq + 1)
                dve.tensor_scalar(var_eps[:, :], mean_var[:, 1:2], NORM_EPS, None, ALU.add).then_inc(var_done, 1)

            def normalise(g, i, j):
                dve.wait_ge(rstd_done, 2 * (g * TILES + i) + j + 1)
                dve.tensor_scalar(z[:, j, :], z[:, j, :], mean_var[:, 0:1], rstd[:, :], ALU.subtract, ALU.mult)\
                    .then_inc(out_done, 1)

            def finish(g, i, t, before):
                for (of_g, of_i), place in ((before, t + TURN), ((g, i), t)):
                    for j in range(2):
                        end = first_part(of_g) if j == 0 else TURN
                        if of_i is not None and place == end + 1 + j:
                            add_up(of_g, of_i, j)
                        if of_i is not None and place == end + 2 + j:
                            normalise(of_g, of_i, j)

            def cols_turn(g, i, before):
                for t in range(TURN):
                    low_part(raw_chunk(t), cols_base(g) + i * TURN + t, cols_slot(t))
                    finish(g, i, t, before)
                    if before[1] is None:
                        if t == 0:
                            degrees(PANELS - 1)
                        if t == 1:
                            save_partial(PANELS - 1, FIRST_CHUNKS)
                        if t == 3:
                            y_low(PANELS - 1)

            for g in range(GROUPS // 2):
                cols_turn(g, 0, (g - 1, TILES - 1) if g > 0 else (0, None))
                if g == 0:
                    cols_turn(0, 1, (0, 0))
                with dve.Fori(2 if g == 0 else 1, TILES) as i:
                    cols_turn(g, i, (g, i - 1))
            for j, step in ((1, add_up), (1, normalise)):
                step(GROUPS // 2 - 1, TILES - 1, j)

        @block.tensor
        def _(pe):
            def fold_sums(p):
                pe.wait_ge(spread_done, p + 1)
                if not isinstance(p, int) or p > 0:
                    pe.wait_ge(deg_done, p)
                pe.matmul(deg_ps[:, 0:1], spread[:, :, :].rearrange("p r c -> p (r c)"), ones[:, :],
                          start=True, stop=True).then_inc(fold_done, 1)

            def x_w(p):
                pe.wait_ge(xt_in, 16 * (p + 1))
                if not isinstance(p, int) or p > 0:
                    pe.wait_ge(y_done, p)
                for h in range(2):
                    ins = pe.matmul(y_ps[:, 0:D], xt_sb[:, h, :], wt_sb[:, h, :], start=h == 0, stop=h == 1)
                ins.then_inc(y_ps_done, 1)

            def multiply(bank, n, slot, c, first, last):
                pe.wait_ge(lo_done, n + 1)
                for t in range(TILES):
                    tile = c * TILES + t
                    cols = slice(t * P, (t + 1) * P)

                    def by_high(stop):
                        return pe.matmul(prod[:, bank, :], hi[:, slot, cols], y[:, tile, :],
                                         start=first and t == 0, stop=stop)

                    def by_low():
                        return pe.matmul(prod[:, bank, D:2 * D], lo[:, slot, cols], y[:, tile, 0:D],
                                         start=False, stop=False)

                    if t < TILES - 1:
                        by_high(False)
                        by_low()
                    else:
                        by_low()
                        by_high(last).then_inc(chunk_used, 1)

            def rows_panel(g, q, with_last):
                p, n0 = g * TILES + q, rows_base(g) + q * rows_chunks(g)
                m = p - TILES
                if with_last and g <= 1:
                    fold_sums(p - 1)
                    x_w(p - 1)
                if g > 0 and (not isinstance(m, int) or m > 1):
                    pe.wait_ge(prod_read, m - 1)
                for t, c in enumerate(rows_order(g)):
                    if c == g - 1:
                        pe.wait_ge(y_done, TILES * g)
                    multiply(p % 2, n0 + t, rows_slot(t, g), c, t == 0, t == g - 1)
                    if g > 1 and t == FOLD_AFTER:
                        fold_sums(p - 1)
                        x_w(p - 1)
                if with_diagonal(g):
                    if not isinstance(m, int) or m > 0:
                        pe.wait_ge(diagonal_read, m)
                    multiply(2, n0 + g, rows_slot(g, g), g - 1, True, True)

            pe.wait_ge(const_in, 32)
            for g in range(GROUPS):
                peeled = 2 if g <= 1 else 0
                for q in range(peeled):
                    rows_panel(g, q, with_last=g + q > 0)
                with pe.Fori(peeled, TILES) as q:
                    rows_panel(g, q, with_last=True)
            fold_sums(PANELS - 1)
            x_w(PANELS - 1)

            for g in range(GROUPS // 2):
                with pe.Fori(0, TILES) as i:
                    for t in range(TURN):
                        j, c = turn_chunk(g, t)
                        if t in (0, first_part(g)):
                            pe.wait_ge(prod_read, FIRST_PANELS + 2 * (g * TILES + i) + j - 1)
                        if c == CHUNKS - 1:
                            pe.wait_ge(y_done, PANELS)
                        multiply(j, cols_base(g) + i * TURN + t, cols_slot(t), c,
                                 t in (0, first_part(g)), c == CHUNKS - 1)


def kernel(x, adj, L0_gnn_W, L0_gnn_b):
    import numpy as _np
    import concourse.bacc as _bacc
    from concourse import mybir as _mybir
    from concourse.bass_utils import run_bass_kernel_spmd as _run

    x, adj, w, b = (_np.asarray(a) for a in (x, adj, L0_gnn_W, L0_gnn_b))
    arrays = {
        "adj_rows": _np.ascontiguousarray(_np.stack([
            adj.reshape(PANELS, ROWGROUPS, Q, CHUNKS, TILES, ROWGROUPS, Q)[:, :, :, chunks]
            for chunks in (list(range(QUARTERS)), list(LATE_CHUNKS))
        ]).transpose(1, 4, 6, 3, 2, 0, 5, 7)).reshape(PANELS, QUARTERS, P, QW),
        "adj_cols": _np.ascontiguousarray(
            adj.reshape(PANELS, P, CHUNKS, TILES, P).transpose(0, 2, 4, 3, 1)
        ).reshape(PANELS, CHUNKS, P, CW),
        "x": _np.ascontiguousarray(x),
        "x_t": _np.ascontiguousarray(x.reshape(PANELS, P, 2, P).transpose(0, 3, 2, 1)),
        "w_t": _np.ascontiguousarray(w.reshape(D, 2, P).transpose(2, 1, 0)),
        "bias": _np.ascontiguousarray(_np.broadcast_to(b, (P, D))),
    }
    nc = _bacc.Bacc("TRN2", target_bir_lowering=False, num_devices=1)
    f32 = _mybir.dt.float32
    ins = {k: nc.dram_tensor(k, a.shape, f32, kind="ExternalInput").ap() for k, a in arrays.items()}
    out = nc.dram_tensor("out", (N, D), f32, kind="ExternalOutput").ap()
    partial = nc.dram_tensor("partial", (PANELS, P, D), f32).ap()
    diagonal = nc.dram_tensor("diagonal", (DIAGONALS, P, D), f32).ap()
    gnn_kernel(nc, out=out, partial=partial, diagonal=diagonal, **ins)
    r = _run(nc, [arrays], core_ids=[0])
    return r.results[0]["out"]
```
